# Optimizing a Trainium2 kernel written in Bass

```python
import numpy as np
import jax
import jax.numpy as jnp

def _softmax(x, axis=-1):
    return jax.nn.softmax(x, axis=axis)

def _gelu(x):
    return jax.nn.gelu(x, approximate=True)

def _silu(x):
    return jax.nn.silu(x)

def _sigmoid(x):
    return jax.nn.sigmoid(x)

def _layernorm(x, axis=-1, eps=1e-05):
    m = jnp.mean(x, axis=axis, keepdims=True)
    v = jnp.var(x, axis=axis, keepdims=True)
    return (x - m) / jnp.sqrt(v + eps)

def _scatter_add(tgt, idx, src, axis=0):
    return tgt.at[idx].add(src)

def _segment_sum(src, seg, n):
    return jax.ops.segment_sum(src, seg, n)
kernel_name = 'mk_macaron_d1_jaxref_r8_19b785'

def setup_inputs(seed: int=0):
    np.random.seed(seed)
    _w = jnp.asarray

    def _L0_attn_setup():
        import jax, jax.numpy as jnp
        from jax import lax
        import numpy as np
        D_MODEL, D_INNER, D_STATE, D_CONV, DT_RANK = (128, 256, 16, 4, 64)
        B, L = (2, 128)
        key = jax.random.key(seed)
        ks = jax.random.split(key, 10)
        s = lambda *sh: 1.0 / np.sqrt(sh[0])
        return {'x': jax.random.normal(ks[0], (B, L, D_MODEL), jnp.float32), 'W_in': jax.random.normal(ks[1], (D_MODEL, 2 * D_INNER), jnp.float32) * s(D_MODEL), 'conv_w': jax.random.normal(ks[2], (D_INNER, D_CONV), jnp.float32) * s(D_CONV), 'conv_b': jax.random.normal(ks[3], (D_INNER,), jnp.float32) * 0.1, 'W_x': jax.random.normal(ks[4], (D_INNER, DT_RANK + 2 * D_STATE), jnp.float32) * s(D_INNER), 'W_dt': jax.random.normal(ks[5], (DT_RANK, D_INNER), jnp.float32) * s(DT_RANK), 'b_dt': jax.random.uniform(ks[6], (D_INNER,), jnp.float32, -4.0, -2.0), 'A_log': jnp.log(jnp.broadcast_to(jnp.arange(1, D_STATE + 1, dtype=jnp.float32), (D_INNER, D_STATE))), 'D_param': jnp.ones((D_INNER,), jnp.float32), 'W_out': jax.random.normal(ks[7], (D_INNER, D_MODEL), jnp.float32) * s(D_INNER)}
    _L0_attn_in = _L0_attn_setup()

    def _L0_ffn_setup():
        import jax, jax.numpy as jnp
        import numpy as np
        B, S, H = (2, 128, 128)
        E, F = (8, 512)
        GATE_TEMP = 0.1
        key = jax.random.key(seed)
        ks = jax.random.split(key, 6)
        s_h = 1.0 / np.sqrt(H)
        s_f = 1.0 / np.sqrt(F)
        return {'hidden_states': jax.random.normal(ks[0], (B, S, H), dtype=jnp.float32), 'w_router': jax.random.normal(ks[1], (H, E), dtype=jnp.float32) * s_h, 'w_gating': jax.random.normal(ks[2], (H, E), dtype=jnp.float32) * s_h, 'w_gate': jax.random.normal(ks[3], (E, H, F), dtype=jnp.float32) * s_h, 'w_up': jax.random.normal(ks[4], (E, H, F), dtype=jnp.float32) * s_h, 'w_down': jax.random.normal(ks[5], (E, F, H), dtype=jnp.float32) * s_f}
    _L0_ffn_in = _L0_ffn_setup()
    _d = {'L0_attn_x': _L0_attn_in['x'], 'L0_attn_W_in': _L0_attn_in['W_in'], 'L0_attn_conv_w': _L0_attn_in['conv_w'], 'L0_attn_conv_b': _L0_attn_in['conv_b'], 'L0_attn_W_x': _L0_attn_in['W_x'], 'L0_attn_W_dt': _L0_attn_in['W_dt'], 'L0_attn_b_dt': _L0_attn_in['b_dt'], 'L0_attn_A_log': _L0_attn_in['A_log'], 'L0_attn_D_param': _L0_attn_in['D_param'], 'L0_attn_W_out': _L0_attn_in['W_out'], 'L0_ffn_w_router': _L0_ffn_in['w_router'], 'L0_ffn_w_gating': _L0_ffn_in['w_gating'], 'L0_ffn_w_gate': _L0_ffn_in['w_gate'], 'L0_ffn_w_up': _L0_ffn_in['w_up'], 'L0_ffn_w_down': _L0_ffn_in['w_down']}
    _x0 = _d['L0_attn_x']
    _d['L0_attn_x'] = jax.random.normal(jax.random.fold_in(jax.random.key(seed), 1), (4, 1024, 128), dtype=_x0.dtype)
    del _x0
    return _d

def reference(L0_attn_x, L0_attn_W_in, L0_attn_conv_w, L0_attn_conv_b, L0_attn_W_x, L0_attn_W_dt, L0_attn_b_dt, L0_attn_A_log, L0_attn_D_param, L0_attn_W_out, L0_ffn_w_router, L0_ffn_w_gating, L0_ffn_w_gate, L0_ffn_w_up, L0_ffn_w_down):

    def _L0_attn_ref(x, W_in, conv_w, conv_b, W_x, W_dt, b_dt, A_log, D_param, W_out):
        import jax, jax.numpy as jnp
        from jax import lax
        import numpy as np
        D_MODEL, D_INNER, D_STATE, D_CONV, DT_RANK = (128, 256, 16, 4, 64)
        B, L = (2, 128)
        b, l, _ = x.shape
        d_inner, d_conv = conv_w.shape
        dt_rank = W_dt.shape[0]
        d_state = A_log.shape[1]
        xz = x @ W_in
        xs, z = jnp.split(xz, 2, axis=-1)
        xp = jnp.pad(xs, ((0, 0), (d_conv - 1, 0), (0, 0))).transpose(0, 2, 1)
        xc = lax.conv_general_dilated(xp, conv_w[:, None, :], (1,), 'VALID', feature_group_count=d_inner, dimension_numbers=('NCH', 'OIH', 'NCH'))
        xc = jax.nn.silu(xc.transpose(0, 2, 1) + conv_b)
        dbl = xc @ W_x
        dt = jax.nn.softplus(dbl[..., :dt_rank] @ W_dt + b_dt)
        Bm = dbl[..., dt_rank:dt_rank + d_state]
        Cm = dbl[..., dt_rank + d_state:]
        A = -jnp.exp(A_log)
        dA = jnp.exp(dt[..., None] * A)
        dBx = (dt * xc)[..., None] * Bm[:, :, None, :]

        def step(h, inp):
            dA_t, dBx_t, C_t = inp
            h = dA_t * h + dBx_t
            y = jnp.einsum('bdn,bn->bd', h, C_t)
            return (h, y)
        h0 = jnp.zeros((b, d_inner, d_state), x.dtype)
        _, ys = lax.scan(step, h0, (dA.transpose(1, 0, 2, 3), dBx.transpose(1, 0, 2, 3), Cm.transpose(1, 0, 2)))
        y = ys.transpose(1, 0, 2) + xc * D_param
        y = y * jax.nn.silu(z)
        return y @ W_out

    def _L0_ffn_ref(hidden_states, w_router, w_gating, w_gate, w_up, w_down):
        import jax, jax.numpy as jnp
        import numpy as np
        B, S, H = (2, 128, 128)
        E, F = (8, 512)
        GATE_TEMP = 0.1
        x = hidden_states
        router_probs = jax.nn.softmax(jnp.einsum('bsh,he->bse', x, w_router), axis=-1)
        gate_weights = jax.nn.softmax(jnp.einsum('bsh,he->bse', x, w_gating) / GATE_TEMP, axis=-1)
        g = jnp.einsum('bsh,ehf->ebsf', x, w_gate)
        u = jnp.einsum('bsh,ehf->ebsf', x, w_up)
        h = jax.nn.silu(g) * u
        expert_out = jnp.einsum('ebsf,efh->ebsh', h, w_down)
        cw = router_probs * gate_weights
        cw = cw / (jnp.sum(cw, axis=-1, keepdims=True) + 1e-09)
        out = jnp.einsum('ebsh,bse->bsh', expert_out, cw)
        return out
    x = L0_attn_x
    x = x + 0.5 * _L0_ffn_ref(_layernorm(x, axis=-1), L0_ffn_w_router, L0_ffn_w_gating, L0_ffn_w_gate, L0_ffn_w_up, L0_ffn_w_down)
    x = x + _L0_attn_ref(_layernorm(x, axis=-1), L0_attn_W_in, L0_attn_conv_w, L0_attn_conv_b, L0_attn_W_x, L0_attn_W_dt, L0_attn_b_dt, L0_attn_A_log, L0_attn_D_param, L0_attn_W_out)
    x = x + 0.5 * _L0_ffn_ref(_layernorm(x, axis=-1), L0_ffn_w_router, L0_ffn_w_gating, L0_ffn_w_gate, L0_ffn_w_up, L0_ffn_w_down)
    return x

_drawn_inputs = setup_inputs


def setup_inputs(seed=0):
    import zlib

    import numpy as np

    out = dict(_drawn_inputs(seed))
    spreads = {'L0_attn_D_param': (1.0, 0.2)}
    factors = {}
    for name, (base, spread) in spreads.items():
        noise = np.random.default_rng([zlib.crc32(name.encode()), seed]).standard_normal(out[name].shape)
        drawn = base * np.exp(spread * noise) if base else spread * noise
        out[name] = jnp.asarray(drawn.astype(out[name].dtype))
    for name, factor in factors.items():
        out[name] = (out[name] * factor).astype(out[name].dtype)
    return out
```

```python
from contextlib import ExitStack

import numpy as np

import concourse.bass as bass
from concourse import mybir

ALU = mybir.AluOpType
ACT = mybir.ActivationFunctionType
AX = mybir.AxisListType
F32 = mybir.dt.float32
F32R = mybir.dt.float32r

P = 128
T = 512
NT = 8
SUB = T // P
E = 8
FC = 4
SLOTS = E * FC
NS = 16
RT = 64
LAG = 3
XR = 4
NA = 3
EPS_LN = 1e-5
EPS_CW = 1e-9

ORDER = [(0, 0), (0, 1), (0, 2), (1, 0), (0, 3), (1, 1), (0, 4), (1, 2), (0, 5), (1, 3),
         (0, 6), (1, 4), (0, 7), (1, 5), (1, 6), (1, 7)]
NPOS = len(ORDER)
MSPAN = 56
MBEGIN = 35

class Stream:

    def __init__(self, sem, step=1):
        self.sem, self.step, self.count = sem, step, 0

    def next(self):
        self.count += self.step
        return (self.sem, self.count)

class Queue:

    def __init__(self):
        self.items, self.met = [], {}

    def wait(self, *marks):
        for m in marks:
            if m is None:
                continue
            sem, value = m
            if self.met.get(id(sem), 0) >= value:
                continue
            self.met[id(sem)] = value
            self.items.append(lambda e, sem=sem, value=value: e.wait_ge(sem, value))

    def do(self, fn, stream=None):
        if stream is None:
            self.items.append(fn)
            return None
        mark = stream.next()
        self.items.append(lambda e, fn=fn, sem=mark[0], k=stream.step: fn(e).then_inc(sem, k))
        return mark

    def play(self, eng):
        for f in self.items:
            f(eng)

def macaron_program(nc, x, W_in, conv_w, conv_b, W_x, W_dt, b_dt, A_log, D_param, W_out,
                    w_router, w_gating, w_gate, w_up, w_down, const, out):
    xf = x.rearrange("b (t j p) d -> (b t) p j d", t=2, j=SUB)
    of = out.rearrange("b (t j p) d -> (b t) p j d", t=2, j=SUB)

    with ExitStack() as ctx:
        def sb(name, shape, dt=F32):
            return ctx.enter_context(nc.sbuf_tensor(name, shape, dt))

        def stream(name, step=1):
            return Stream(ctx.enter_context(nc.semaphore(name)), step)

        WG = sb("WG", [P, 2, E, T], F32R)
        WU = sb("WU", [P, 2, E, T], F32R)
        WD = sb("WD", [P, 2, E, FC, P], F32R)
        WI = sb("WI", [P, 2, T], F32R)
        WX = sb("WX", [P, 2, 2, 96], F32R)
        WT = sb("WT", [P, 2, 256], F32R)
        WO = sb("WO", [P, 2, 2, P], F32R)
        WR = sb("WR", [P, 16])
        CON = sb("CON", [P, P + NS * 2 + E])
        SEL = sb("SEL", [P, NS * 2 + E], F32R)
        cw_t = sb("cw_t", [P, 2, 4])
        cb_t = sb("cb_t", [P, 2])
        bdt_t = sb("bdt_t", [P, 2])
        d_t = sb("d_t", [P, 2])

        aneg = sb("aneg", [P, 2, NS])
        mhalf = sb("mhalf", [P, SUB])
        XT = sb("XT", [P, XR, SUB, P])
        XN = sb("XN", [P, SUB, P])
        XF = sb("XF", [P, 2, T])
        XH = sb("XH", [P, 2, 2, T], F32R)
        XC = sb("XC", [P, 2, 2, T], F32R)
        XCF = sb("XCF", [P, T])
        CW = sb("CW", [P, 2, T], F32R)
        HB = sb("HB", [P, 3, T])
        HH = sb("HH", [P, 3, T], F32R)
        HL = sb("HL", [P, 3, T], F32R)
        stats = sb("stats", [P, SUB, 6])
        mv = sb("mv", [P, SUB, 2])
        rs = sb("rs", [P, SUB])
        ve = sb("ve", [P, SUB])
        lg = sb("lg", [P, SUB, 2, E])
        mx = sb("mx", [P, SUB, 2])
        zz = sb("zz", [P, SUB, 2])
        pq = sb("pq", [P, SUB, E])
        sm = sb("sm", [P, SUB])

        cwhl = sb("cwhl", [P, SUB, 2, E])
        RM = sb("RM", [P, 4, T], F32R)
        DTI = RM[:, 3, :]
        BC = sb("BC", [P, T], F32R)
        XS = sb("XS", [P, 2, T + 4])
        HT = sb("HT", [P, 2, 3])
        SZ = sb("SZ", [P, 2, T])
        Y = sb("Y", [P, 2, T])
        DX = sb("DX", [P, 2, T])
        DA = sb("DA", [P, NA, 2, T])
        HS = sb("HS", [P, 2, 2, T])
        car = sb("car", [P, 2, NS])
        PS = ctx.enter_context(nc.psum_tensor("PS", [P, 8, T], F32))
        ident = CON[:, 0:P]

        S = {}
        for n in ("c_small c_x0 c_x1 c_x2 c_x3 "
                  "o_x0 o_x1 o_x2 o_x3").split():
            S[n] = stream(n, 16)
        for e in range(E):
            for k in "gud":
                S[f"c_w{k}{e}"] = stream(f"c_w{k}{e}", 16)
        for n in ("init wh wl g u dn tz m_tr m_lg m_ct m_cb m_win m_wx m_wt m_b m_c m_wo "
                  "a_sil a_hi a_cwh a_acc a_xh a_exp a_cwt a_win a_conv a_xch a_dbl a_sp a_da a_yh a_set "
                  "v_h v_xcf v_ln v_xn v_xf v_sm v_cw v_add v_set v_halo v_cv v_lo v_dt v_dx v_db v_sc v_car v_hc v_yz "
                  "p_lo p_cwl p_pow p_xl p_xcl p_y p_yl p_dx p_set").split():
            S[n] = stream(n)

        PE, VE, SC, GP, SY = (Queue() for _ in range(5))

        ring = {"n": 0, "free": [None, None, None]}

        def bank():
            b = ring["n"] % 3
            ring["n"] += 1
            PE.wait(*(ring["free"][b] or ()))
            ring["free"][b] = None
            return b, PS[:, 5 + b, :]

        def release(b, *marks):
            ring["free"][b] = marks

        def mm(outp, terms, s):
            mark = None
            for k, (l, r) in enumerate(terms):
                first, last = k == 0, k == len(terms) - 1
                mark = PE.do(lambda e, l=l, r=r, f=first, z=last: e.matmul(outp, l, r, start=f, stop=z),
                             S[s] if last else None)
            return mark

        def tt(q, o, a, b, op, s):
            return q.do(lambda e: e.tensor_tensor(o, a, b, op), S[s])

        def ts(q, o, a, s1, s2, op0, op1, s):
            if op1 is None:
                return q.do(lambda e: e.tensor_scalar(o, a, s1, None, op0), S[s])
            return q.do(lambda e: e.tensor_scalar(o, a, s1, s2, op0, op1), S[s])

        def act(o, a, f, s, **kw):
            return SC.do(lambda e: e.activation(o, a, f, **kw), S[s])

        def f32(ap):
            return ap.bitcast(F32)

        XTfree = [[] for _ in range(XR)]

        def load_x(t):
            b = t % XR
            SY.wait(*XTfree[b])
            return SY.do(lambda e: e.dma_start(XT[:, b, :, :], xf[t]), S[f"c_x{b}"])

        x_in = {0: load_x(0)}
        small = None
        stI = DA[:, 0, 0, :]
        stX = DA[:, 0, 1, 0:192].rearrange("p (k n) -> p k n", k=2)
        stT = DA[:, 0, 1, 192:448]
        stO = DA[:, 1, 0, 0:256].rearrange("p (k n) -> p k n", k=2)
        for dst, src in ((CON[:, :], const), (WR[:, 0:E], w_router), (WR[:, E:2 * E], w_gating)):
            small = SY.do(lambda e, dst=dst, src=src: e.dma_start(dst, src), S["c_small"])
        first_small = small

        def stage(e, k):
            s = e % 4
            if s < 2:
                return HS[:, s, 0, :] if k == 0 else (HS[:, s, 1, :] if k == 1 else DX[:, s, :])
            return SZ[:, s - 2, :] if k == 0 else (Y[:, s - 2, :] if k == 1 else XS[:, s - 2, 0:T])

        st_free = {}
        w_in_mark = {}

        def load_w(e):
            for k, (n, src) in enumerate((("g", w_gate[e]), ("u", w_up[e]), ("d", w_down[e].rearrange("(c p) n -> p c n", p=P)))):
                SY.wait(st_free.get((e - 4, k)))
                dst = stage(e, k)
                if k == 2:
                    dst = dst.rearrange("p (c n) -> p c n", c=FC)
                w_in_mark[e, k] = SY.do(lambda q, dst=dst, src=src: q.dma_start(dst, src), S[f"c_w{n}{e}"])

        w_mark = {}

        def split_w(e):
            for k, W in enumerate((WG, WU, WD)):
                src = stage(e, k)
                if k == 2:
                    hi = WD[:, 0, e, :, :].rearrange("p c n -> p (c n)")
                    lo = WD[:, 1, e, :, :].rearrange("p c n -> p (c n)")
                else:
                    hi, lo = W[:, 0, e, :], W[:, 1, e, :]
                VE.wait(w_in_mark[e, k])
                h = VE.do(lambda q, hi=hi, src=src: q.tensor_copy(hi, src), S["wh"])
                VE.wait(h)
                w_mark[e, k] = tt(VE, lo, src, f32(hi), ALU.subtract, "wl")
                st_free[e, k] = w_mark[e, k]

        for e in range(4):
            load_w(e)

        def load_small():
            nonlocal small
            loads = [(stI, W_in), (stX, W_x.rearrange("(k p) n -> p k n", p=P)),
                     (stT[0:RT, :], W_dt), (stT[RT:2 * RT, :], W_dt),
                     (stO, W_out.rearrange("(k p) n -> p k n", p=P)),
                     (cw_t[:, :, :], conv_w.rearrange("(k p) n -> p k n", p=P)),
                     (aneg[:, :, :], A_log.rearrange("(k p) n -> p k n", p=P))]
            for dst, v in ((cb_t, conv_b), (bdt_t, b_dt), (d_t, D_param)):
                loads += [(dst[:, k:k + 1], v.rearrange("(k p o) -> k p o", p=P, o=1)[k]) for k in range(2)]
            for dst, src in loads:
                small = SY.do(lambda e, dst=dst, src=src: e.dma_start(dst, src), S["c_small"])

        VE.do(lambda e: e.memset(mhalf[:, :], -0.5), S["init"])
        VE.do(lambda e: e.memset(f32(BC[0:64, :]), 0.0), S["init"])
        init = VE.do(lambda e: e.memset(f32(CW[:, :, :]), 0.0), S["init"])
        VE.wait(first_small)
        sel_mark = VE.do(lambda e: e.tensor_copy(SEL[:, :], CON[:, P:P + 2 * NS + E]), S["init"])

        def setup_mamba():
            VE.wait(small)
            for hi, lo, src in ((WI[:, 0, :], WI[:, 1, :], stI), (WX[:, :, 0, :], WX[:, :, 1, :], stX),
                                (WT[:, 0, :], WT[:, 1, :], stT), (WO[:, :, 0, :], WO[:, :, 1, :], stO)):
                h = VE.do(lambda q, hi=hi, src=src: q.tensor_copy(hi, src), S["v_set"])
                VE.wait(h)
                l = tt(VE, lo, src, f32(hi), ALU.subtract, "v_set")
                yield
            SC.wait(small)
            a = act(aneg[:, :, :], aneg[:, :, :], ACT.Exp, "a_set")
            VE.wait(a)
            st["m_ready"] = ts(VE, aneg[:, :, :], aneg[:, :, :], -1.0, None, ALU.mult, None, "v_set")
            yield

        st = {}
        XNfree = [None]
        lock = [False]
        tiny = {}

        def norm_transposed(b, xmark):
            while lock[0]:
                yield
            lock[0] = True
            VE.wait(*xmark)
            for j in range(SUB):
                m = VE.do(lambda e, j=j: e.bn_stats(stats[:, j, :], XT[:, b, j, :]), S["v_ln"])
            VE.wait(m)
            for j in range(SUB):
                m = VE.do(lambda e, j=j: e.bn_aggr(mv[:, j, :], stats[:, j, :]), S["v_ln"])
            VE.wait(m)
            m = ts(VE, ve[:, :], mv[:, :, 1], EPS_LN, None, ALU.add, None, "v_ln")
            GP.wait(m, init)
            m = tt(GP, rs[:, :], ve[:, :], mhalf[:, :], ALU.pow, "p_pow")
            yield
            VE.wait(m, XNfree[0])
            for j in range(SUB):
                m = VE.do(lambda e, j=j: e.tensor_scalar(XN[:, j, :], XT[:, b, j, :], mv[:, j, 0:1], rs[:, j:j + 1],
                                                         ALU.subtract, ALU.mult), S["v_xn"])
            lock[0] = False
            bk, ps = bank()
            PE.wait(m, first_small)
            for j in range(SUB):
                t = PE.do(lambda e, j=j: e.transpose(ps[:, j * P:(j + 1) * P], XN[:, j, :], ident), S["m_tr"])
            XNfree[0] = t
            yield
            return bk, ps, t

        prepared = {}
        xh_free = [None, None]
        xf_free = [None, None]
        cw_free = [None, None]

        def prep(p, b, xmark):
            k = p % 2
            bk, ps, t = yield from norm_transposed(b, xmark)
            VE.wait(t, xf_free[k])
            mf = VE.do(lambda e, ps=ps: e.tensor_copy(XF[:, k, :], ps), S["v_xf"])
            release(bk, mf)
            SC.wait(mf, xh_free[k])
            mh = act(XH[:, k, 0, :], XF[:, k, :], ACT.Copy, "a_xh")
            GP.wait(mh, mf)
            ml = tt(GP, XH[:, k, 1, :], XF[:, k, :], f32(XH[:, k, 0, :]), ALU.subtract, "p_xl")
            yield
            bk, ps = bank()
            PE.wait(mf)
            for j in range(SUB):
                t = PE.do(lambda e, j=j, ps=ps: e.matmul(ps[:, j * 16:j * 16 + 16], XF[:, k, j * P:(j + 1) * P], WR[:, :],
                                                         start=True, stop=True), S["m_lg"])
            l4 = ps[:, 0:SUB * 16].rearrange("p (j g e) -> p j g e", j=SUB, g=2)
            VE.wait(t)
            m = VE.do(lambda e: e.tensor_reduce(mx[:, :, :], l4, AX.X, ALU.max), S["v_sm"])
            VE.wait(m)
            m = tt(VE, lg[:, :, :, :], l4, mx[:, :, :].unsqueeze(3).broadcast_to([P, SUB, 2, E]), ALU.subtract, "v_sm")
            release(bk, m)
            yield
            SC.wait(m)
            act(lg[:, :, 0, :], lg[:, :, 0, :], ACT.Exp, "a_exp")
            m = act(lg[:, :, 1, :], lg[:, :, 1, :], ACT.Exp, "a_exp", scale=10.0)
            yield
            VE.wait(m)
            m = VE.do(lambda e: e.tensor_reduce(zz[:, :, :], lg[:, :, :, :], AX.X, ALU.add), S["v_sm"])
            VE.wait(m)
            m = VE.do(lambda e: e.reciprocal(zz[:, :, :], zz[:, :, :]), S["v_sm"])
            VE.wait(m)
            m = tt(VE, lg[:, :, :, :], lg[:, :, :, :], zz[:, :, :].unsqueeze(3).broadcast_to([P, SUB, 2, E]), ALU.mult, "v_sm")
            yield
            VE.wait(m)
            m = tt(VE, pq[:, :, :], lg[:, :, 0, :], lg[:, :, 1, :], ALU.mult, "v_sm")
            VE.wait(m)
            m = VE.do(lambda e: e.tensor_reduce(sm[:, :], pq[:, :, :], AX.X, ALU.add), S["v_sm"])
            VE.wait(m)
            m = ts(VE, sm[:, :], sm[:, :], EPS_CW, 2.0, ALU.add, ALU.mult, "v_sm")
            yield
            VE.wait(m)
            m = VE.do(lambda e: e.reciprocal(sm[:, :], sm[:, :]), S["v_sm"])
            VE.wait(m)
            m = tt(VE, pq[:, :, :], pq[:, :, :], sm[:, :].unsqueeze(2).broadcast_to([P, SUB, E]), ALU.mult, "v_sm")
            yield
            VE.wait(m, tiny.get("cwhl"))
            m = VE.do(lambda e: e.tensor_copy(cwhl[:, :, 0, :].bitcast(F32R), pq[:, :, :]), S["v_sm"])
            VE.wait(m)
            m = tt(VE, cwhl[:, :, 1, :].bitcast(F32R), pq[:, :, :], cwhl[:, :, 0, :], ALU.subtract, "v_cw")
            yield
            bk, ps = bank()
            PE.wait(m)
            for j in range(SUB):
                t = PE.do(lambda e, j=j, ps=ps: e.transpose(ps[0:16, j * P:(j + 1) * P],
                                                            cwhl[:, j, :, :].rearrange("p g e -> p (g e)"), ident), S["m_ct"])
            tiny["cwhl"] = t
            SC.wait(t, cw_free[k], init)
            m = act(CW[0:16, k, :], ps[0:16, :], ACT.Copy, "a_cwt")
            release(bk, m)
            prepared[p] = (mh, ml, m)
            yield

        xc_free = [None, None]
        xc_mark = {}
        xcf_free = [None]

        def scale_x(g):
            p, e = divmod(g, E)
            k, b2 = p % 2, g % 2
            bk, ps = bank()
            PE.wait(prepared[p][2], sel_mark)
            t = PE.do(lambda q: q.matmul(ps, SEL[:, 2 * NS + e:2 * NS + e + 1].broadcast_to([P, P]), CW[:, k, :],
                                         start=True, stop=True), S["m_cb"])
            cw_free[k] = t
            VE.wait(t, xcf_free[0])
            m = tt(VE, XCF[:, :], ps, XF[:, k, :], ALU.mult, "v_xcf")
            release(bk, m)
            xf_free[k] = m
            SC.wait(m, xc_free[b2])
            h = act(XC[:, b2, 0, :], XCF[:, :], ACT.Copy, "a_cwh")
            GP.wait(h, m, xc_free[b2])
            l = tt(GP, XC[:, b2, 1, :], XCF[:, :], f32(XC[:, b2, 0, :]), ALU.subtract, "p_cwl")
            xcf_free[0] = l
            xc_mark[g] = (h, l)

        hist = {}
        acc_free = [None]

        def tail(p):
            kind, t = ORDER[p]
            b = t % XR
            SC.wait(hist[p * SLOTS + SLOTS - 1]["dn"], XNfree[0])
            A = XN[:, :, :].rearrange("p j d -> p (j d)")
            m = act(A, PS[:, 4, :], ACT.Copy, "a_acc")
            acc_free[0] = m
            bk, ps = bank()
            PE.wait(m)
            for j in range(SUB):
                tr = PE.do(lambda e, j=j: e.transpose(ps[:, j * P:(j + 1) * P], A[:, j * P:(j + 1) * P], ident), S["tz"])
            XNfree[0] = tr
            VE.wait(tr)
            m = tt(VE, XT[:, b, :, :].rearrange("p j d -> p (j d)"), XT[:, b, :, :].rearrange("p j d -> p (j d)"),
                   ps, ALU.add, "v_add")
            release(bk, m)
            if kind == 0:
                st["x1", t] = m
            else:
                SY.wait(m)
                o = SY.do(lambda e: e.dma_start(of[t], XT[:, b, :, :]), S[f"o_x{b}"])
                XTfree[b] = [o]
                outs.append(o)

        outs = []

        def first(i):
            p, r = divmod(i, SLOTS)
            e, c = divmod(r, FC)
            k = p % 2
            G, U = PS[:, i % 2, :], PS[:, 2 + i % 2, :]
            h = hist.setdefault(i, {})
            old = hist.get(i - 2)
            wg = [WG[:, s, e, c * P:(c + 1) * P] for s in (0, 1)]
            wu = [WU[:, s, e, c * P:(c + 1) * P] for s in (0, 1)]
            PE.wait(w_mark[e, 0], w_mark[e, 1], prepared[p][0], prepared[p][1])
            if old:
                PE.wait(old["sil"])
            xh, xl = XH[:, k, 0, :], XH[:, k, 1, :]
            h["g"] = mm(G, [(wg[0], xh), (wg[0], xl), (wg[1], xh)], "g")
            b2 = (p * E + e) % 2
            PE.wait(*xc_mark[p * E + e])
            if old:
                PE.wait(old["h"])
            xh, xl = XC[:, b2, 0, :], XC[:, b2, 1, :]
            h["u"] = mm(U, [(wu[0], xh), (wu[0], xl), (wu[1], xh)], "u")
            xc_free[b2] = h["u"]
            xh_free[k] = h["g"]
            H = HB[:, i % 3, :]
            if i >= 3:
                SC.wait(hist[i - 3]["lo"])
            SC.wait(h["g"])
            h["sil"] = act(H, G, ACT.Silu, "a_sil")
            VE.wait(h["sil"], h["u"])
            h["h"] = tt(VE, H, U, H, ALU.mult, "v_h")

        def parts(i):
            h = hist[i]
            H = HB[:, i % 3, :]
            old = hist.get(i - 3)
            SC.wait(h["h"])
            if old:
                SC.wait(old["dn"])
                GP.wait(old["dn"])
            h["hi"] = act(HH[:, i % 3, :], H, ACT.Copy, "a_hi")
            GP.wait(h["h"], h["hi"])
            h["lo"] = tt(GP, HL[:, i % 3, :], H, f32(HH[:, i % 3, :]), ALU.subtract, "p_lo")

        def down(i):
            p, r = divmod(i, SLOTS)
            e, c = divmod(r, FC)
            h = hist[i]
            wh, wl = WD[:, 0, e, c, :], WD[:, 1, e, c, :]
            hh, hl = HH[:, i % 3, :], HL[:, i % 3, :]
            A = PS[:, 4, :]
            a, z = r == 0, r == SLOTS - 1
            if a:
                PE.wait(acc_free[0])
            PE.wait(w_mark[e, 2], h["hi"])
            PE.do(lambda q: q.matmul(A, wh, hh, start=a, stop=False))
            PE.do(lambda q: q.matmul(A, wl, hh, start=False, stop=False))
            PE.wait(h["lo"])
            h["dn"] = PE.do(lambda q: q.matmul(A, wh, hl, start=False, stop=z), S["dn"])

        mfree = {}

        def mamba(t):
            b = t % XR
            start = t % 2 == 0
            if t == 0:
                yield from setup_mamba()
                PE.wait(st["m_ready"])
                SC.wait(st["m_ready"])
            bk, ps, tr = yield from norm_transposed(b, [st["x1", t]])
            SC.wait(tr, mfree.get("RM"))
            mh = act(RM[:, 0, :], ps, ACT.Copy, "a_xh")
            VE.wait(mh, tr)
            ml = tt(VE, RM[:, 1, :], ps, f32(RM[:, 0, :]), ALU.subtract, "v_lo")
            release(bk, mh, ml)
            if start:
                VE.do(lambda e: e.memset(XS[:, :, 0:3], 0.0), S["v_halo"])
                ch = VE.do(lambda e: e.memset(car[:, :, :], 0.0), S["v_halo"])
            else:
                ch = VE.do(lambda e: e.tensor_copy(XS[:, :, 0:3], HT[:, :, :]), S["v_halo"])
            yield
            for j in range(4):
                bk, ps = bank()
                PE.wait(mh, ml)
                w = [WI[:, s, j * P:(j + 1) * P] for s in (0, 1)]
                tm = mm(ps, [(w[0], RM[:, 0, :]), (w[0], RM[:, 1, :]), (w[1], RM[:, 0, :])], "m_win")
                SC.wait(tm)
                if j < 2:
                    SC.wait(mfree.get("DT"))
                    m = act(XS[:, j, 3:3 + T], ps, ACT.Copy, "a_win")
                    xs_m = m
                else:
                    SC.wait(mfree.get("SZ"))
                    m = act(SZ[:, j - 2, :], ps, ACT.Silu, "a_win")
                release(bk, m)
                yield
            sz_m = m
            VE.wait(xs_m, ch)
            hm = VE.do(lambda e: e.tensor_copy(HT[:, :, :], XS[:, :, T:T + 3]), S["v_halo"])
            xcm = []
            for j in range(2):
                VE.wait(mfree.get("Y"))
                m = ts(VE, Y[:, j, :], XS[:, j, 0:T], cw_t[:, j, 0:1], None, ALU.mult, None, "v_cv")
                for q in range(1, 4):
                    yield
                    VE.wait(m)
                    m = VE.do(lambda e, j=j, q=q: e.scalar_tensor_tensor(
                        out=Y[:, j, :], in0=XS[:, j, q:q + T], scalar=cw_t[:, j, q:q + 1], in1=Y[:, j, :],
                        op0=ALU.mult, op1=ALU.add), S["v_cv"])
                SC.wait(m)
                m = act(Y[:, j, :], Y[:, j, :], ACT.Silu, "a_conv", bias=cb_t[:, j:j + 1])
                SC.wait(m)
                if j == 0:
                    SC.wait(tm)
                mh = act(RM[:, 2 * j, :], Y[:, j, :], ACT.Copy, "a_xch")
                GP.wait(m, mh, tm)
                ml = tt(GP, RM[:, 2 * j + 1, :], Y[:, j, :], f32(RM[:, 2 * j, :]), ALU.subtract, "p_xcl")
                xcm.append(m)
                yield
            bk, ps = bank()
            PE.wait(mh, ml)
            terms = []
            for j in range(2):
                w = [WX[:, j, s, :] for s in (0, 1)]
                terms += [(w[0], RM[:, 2 * j, :]), (w[0], RM[:, 2 * j + 1, :]), (w[1], RM[:, 2 * j, :])]
            tm = mm(ps[0:96, :], terms, "m_wx")
            SC.wait(tm, mfree.get("BC"))
            m1 = act(DTI[0:RT, :], ps[0:RT, :], ACT.Copy, "a_dbl")
            m2 = act(BC[64:96, :], ps[64:96, :], ACT.Copy, "a_dbl")
            VE.wait(m1, m2, tm)
            m3 = tt(VE, DTI[RT:2 * RT, :], ps[0:RT, :], f32(DTI[0:RT, :]), ALU.subtract, "v_lo")
            m4 = tt(VE, BC[96:128, :], ps[64:96, :], f32(BC[64:96, :]), ALU.subtract, "v_lo")
            release(bk, m2, m4)
            yield
            pend = []
            for j in range(2):
                bk, ps = bank()
                PE.wait(m1, m3)
                tm = mm(ps, [(WT[:, s, j * P:(j + 1) * P], DTI[:, :]) for s in (0, 1)], "m_wt")
                mfree["DTI"] = tm
                SC.wait(tm, mfree.get("DX"))
                a = act(DX[:, j, :], ps, ACT.Abs, "a_sp", bias=bdt_t[:, j:j + 1])
                VE.wait(tm, a)
                r = ts(VE, XS[:, j, 3:3 + T], ps, bdt_t[:, j:j + 1], 0.0, ALU.add, ALU.max, "v_dt")
                release(bk, a, r)
                pend.append((a, r))
                yield
            SC.wait(pend[1][0])
            a = act(DX[:, :, :], DX[:, :, :], ACT.Exp, "a_sp", scale=-1.0)
            SC.wait(a)
            a = act(DX[:, :, :], DX[:, :, :], ACT.Ln, "a_sp", bias=1.0)
            yield
            VE.wait(a, pend[1][1])
            dt = XS[:, :, 3:3 + T]
            dtm = tt(VE, dt, dt, DX[:, :, :], ALU.add, "v_dt")
            VE.wait(dtm, *xcm)
            dxm = tt(VE, DX[:, :, :], dt, Y[:, :, :], ALU.mult, "v_dx")
            yield
            VE.wait(dxm)
            GP_y = None
            for j in range(2):
                ym = ts(VE, Y[:, j, :], Y[:, j, :], d_t[:, j:j + 1], None, ALU.mult, None, "v_dx")
            GP_y = ym
            yield

            da, sc, py = {}, {}, {}

            def decay(n):
                SC.wait(dtm, mfree.get(("DA", n % NA)))
                for j in range(2):
                    m = act(DA[:, n % NA, j, :], XS[:, j, 3:3 + T], ACT.Exp, "a_da", scale=aneg[:, j, n:n + 1])
                da[n] = m

            for n in range(NA):
                decay(n)
                yield
            for n in range(NS):
                H = HS[:, n % 2, :, :]
                bb, pb = bank()
                PE.wait(m2, m4)
                tb = PE.do(lambda e, n=n, pb=pb: e.matmul(pb, SEL[:, n:n + 1].broadcast_to([P, P]), BC[:, :],
                                                         start=True, stop=True), S["m_b"])
                VE.wait(tb, dxm, mfree.get(("HS", n % 2)))
                m = tt(VE, H, pb.unsqueeze(1).broadcast_to([P, 2, T]), DX[:, :, :], ALU.mult, "v_db")
                release(bb, m)
                yield
                VE.wait(m, da[n])
                for j in range(2):
                    m = VE.do(lambda e, n=n, j=j, H=H: e.tensor_tensor_scan(
                        H[:, j, :], DA[:, n % NA, j, :], H[:, j, :], car[:, j, n:n + 1], ALU.mult, ALU.add), S["v_sc"])
                mfree["DA", n % NA] = m
                bb, pb = bank()
                tb = PE.do(lambda e, n=n, pb=pb: e.matmul(pb, SEL[:, NS + n:NS + n + 1].broadcast_to([P, P]), BC[:, :],
                                                         start=True, stop=True), S["m_c"])
                mfree["BC"] = tb
                if n + NA < NS:
                    decay(n + NA)
                yield
                VE.wait(m, tb)
                cm = VE.do(lambda e, n=n, H=H: e.tensor_copy(car[:, :, n], H[:, :, T - 1]), S["v_car"])
                VE.wait(cm)
                m = tt(VE, H, pb.unsqueeze(1).broadcast_to([P, 2, T]), H, ALU.mult, "v_hc")
                release(bb, m)
                GP.wait(m, GP_y)
                GP_y = tt(GP, Y[:, :, :], Y[:, :, :], H, ALU.add, "p_y")
                mfree["HS", n % 2] = GP_y
                yield
            mfree["DT"] = mfree["DA", (NS - 1) % NA]
            SC_last = da[NS - 1]
            mfree["DTA"] = SC_last
            mfree["DX"] = m
            VE.wait(GP_y, sz_m)
            m = tt(VE, Y[:, :, :], Y[:, :, :], SZ[:, :, :], ALU.mult, "v_yz")
            mfree["SZ"] = m
            yield
            for j in range(2):
                SC.wait(m)
                mh = act(RM[:, 2 * j, :], Y[:, j, :], ACT.Copy, "a_yh")
                GP.wait(mh, m, mfree["DTI"])
                ml = tt(GP, RM[:, 2 * j + 1, :], Y[:, j, :], f32(RM[:, 2 * j, :]), ALU.subtract, "p_yl")
                yield
            mfree["Y"] = ml
            bk, ps = bank()
            PE.wait(mh, ml)
            for s4 in range(SUB):
                terms = []
                for j in range(2):
                    yh = RM[:, 2 * j, s4 * P:(s4 + 1) * P]
                    yl = RM[:, 2 * j + 1, s4 * P:(s4 + 1) * P]
                    terms += [(yh, WO[:, j, 0, :]), (yl, WO[:, j, 0, :]), (yh, WO[:, j, 1, :])]
                tm = mm(ps[:, s4 * P:(s4 + 1) * P], terms, "m_wo")
            mfree["RM"] = tm
            yield
            VE.wait(tm)
            X = XT[:, b, :, :].rearrange("p j d -> p (j d)")
            m = tt(VE, X, X, ps, ALU.add, "v_add")
            release(bk, m)
            st["x2", t] = m
            yield

        def run(gen, n=10 ** 9):
            for _ in range(n):
                if next(gen, "end") == "end":
                    return True
            return False

        def xmark(p):
            kind, t = ORDER[p]
            return [x_in[t]] if kind == 0 else [st["x2", t]]

        run(prep(0, 0, [x_in[0]]))
        split_w(0)
        scale_x(0)
        total = NPOS * SLOTS
        mg = None
        mt = 0
        msteps = {}
        pg = None
        MLEN = 80

        def m_advance(i):
            nonlocal mg, mt
            while mt < NT:
                begin = MBEGIN + MSPAN * mt
                due = (i - begin + 1) * MLEN // (MSPAN - 1)
                if i < begin:
                    return
                if mg is None:
                    if ("x1", mt) not in st:
                        return
                    mg = mamba(mt)
                    msteps[mt] = 0
                while msteps[mt] < due:
                    msteps[mt] += 1
                    if run(mg, 1):
                        mg = None
                        mt += 1
                        break
                if mg is not None:
                    return

        for i in range(total):
            p, r = divmod(i, SLOTS)
            first(i)
            if i >= 1:
                parts(i - 1)
            if i >= LAG:
                down(i - LAG)
                if r == LAG - 1 and p > 0:
                    tail(p - 1)
            if p == 0:
                if r % 4 == 0 and r // 4 + 1 < E:
                    split_w(r // 4 + 1)
                    if r // 4 + 4 < E:
                        load_w(r // 4 + 4)
                if r == 6:
                    load_small()
            if r == 4 and p + 1 < NPOS and ORDER[p + 1][0] == 0:
                t = ORDER[p + 1][1]
                x_in[t] = load_x(t)
            if r % 4 == 1 and i // 4 + 1 < NPOS * E:
                if r // 4 == E - 1:
                    while pg is not None and not run(pg, 1):
                        pass
                    pg = None
                scale_x(i // 4 + 1)
            m_advance(i)
            if p + 1 < NPOS and r >= 16:
                if r == 16:
                    kind, t = ORDER[p + 1]
                    pg = "due"
                if pg == "due":
                    kind, t = ORDER[p + 1]
                    if kind == 0 or ("x2", t) in st:
                        pg = prep(p + 1, t % XR, xmark(p + 1))
                    elif r == 28:
                        while ("x2", t) not in st:
                            m_advance(i + 10 ** 6)
                        pg = prep(p + 1, t % XR, xmark(p + 1))
                if pg not in (None, "due"):
                    run(pg, 1)
        parts(total - 1)
        for i in range(total - LAG, total):
            down(i)
        tail(NPOS - 1)
        for o in outs:
            SY.wait(o)

        block = ctx.enter_context(nc.Block())

        @block.sync
        def _(eng):
            SY.play(eng)

        @block.tensor
        def _(eng):
            PE.play(eng)

        @block.vector
        def _(eng):
            VE.play(eng)

        @block.scalar
        def _(eng):
            SC.play(eng)

        @block.gpsimd
        def _(eng):
            GP.play(eng)

_INS = ['L0_attn_x', 'L0_attn_W_in', 'L0_attn_conv_w', 'L0_attn_conv_b', 'L0_attn_W_x', 'L0_attn_W_dt', 'L0_attn_b_dt',
        'L0_attn_A_log', 'L0_attn_D_param', 'L0_attn_W_out', 'L0_ffn_w_router', 'L0_ffn_w_gating', 'L0_ffn_w_gate',
        'L0_ffn_w_up', 'L0_ffn_w_down']

def _constants():
    c = np.zeros((P, P + 2 * NS + E), np.float32)
    c[:, :P] = np.eye(P)
    for n in range(2 * NS):
        c[64 + n, P + n] = 1.0
        c[96 + n, P + n] = 1.0
    for e in range(E):
        c[e, P + 2 * NS + e] = 1.0
        c[E + e, P + 2 * NS + e] = 1.0
    return c

def kernel(**inputs):
    import concourse.bacc as _bacc
    from concourse.bass_utils import run_bass_kernel_spmd as _run

    nc = _bacc.Bacc("TRN2", target_bir_lowering=False, num_devices=1)
    arrays, args = {}, []
    for name in _INS:
        a = np.ascontiguousarray(inputs[name])
        arrays[f"in_{name}_dram"] = a
        args.append(nc.dram_tensor(f"in_{name}_dram", a.shape, mybir.dt.from_np(a.dtype), kind="ExternalInput").ap())
    c = _constants()
    arrays["in_const_dram"] = c
    args.append(nc.dram_tensor("in_const_dram", c.shape, F32, kind="ExternalInput").ap())
    args.append(nc.dram_tensor("out_0_dram", (4, 1024, P), F32, kind="ExternalOutput").ap())
    macaron_program(nc, *args)
    r = _run(nc, [arrays], core_ids=[0])
    return r.results[0]["out_0_dram"]
```

```python
from contextlib import ExitStack

import numpy as np

import concourse.bass as bass
from concourse import mybir

ALU = mybir.AluOpType
ACT = mybir.ActivationFunctionType
AX = mybir.AxisListType
F32 = mybir.dt.float32
F32R = mybir.dt.float32r

P = 128
T = 512
NT = 8
SUB = T // P
E = 8
FC = 4
SLOTS = E * FC
NS = 16
RT = 64
LAG = 3
NH = LAG + 1
XR = 5
NA = 2
EPS_LN = 1e-5
EPS_CW = 1e-9

ORDER = [(0, 0), (0, 1), (0, 2), (0, 3), (1, 0), (0, 4), (1, 1), (0, 5), (1, 2), (0, 6), (1, 3), (0, 7), (1, 4), (1, 5), (1, 6), (1, 7)]
NPOS = len(ORDER)
BEGIN = 34
RATE = 1.4
PLAIN = (0, NPOS - 1)
PREP = 10
PLIM = 3.0
DIFF = 0.0
XLIM = 3.0
SLOT_WEIGHT = 2.3
MAXC = 3.0
LOADR = 7
BRATE = 1.0
COST = {"v_h": .6, "v_g": .6, "v_xcf": .6, "v_sc": .63, "v_db": 1.13, "v_hc": 1.13, "v_xn": .2, "v_ln": .1, "v_add": .6,
        "v_lo": .6, "v_dt": .7, "wl": .6, "v_z": .6, "v_cv": .5, "v_xf": .6, "v_yz": 1.13, "v_dx": .39, "v_set": .6,
        "v_sm": .1, "v_car": .07, "v_cwl": .6,
        "p_h": 1.22, "p_y": 1.22, "p_cwl": 1.22, "p_pow": .96, "p_xl": 1.22, "p_xcl": 1.22, "p_yl": 1.22, "p_dx": 2.3,
        "a_xn": .3, "a_xf": .48, "a_cv": .61, "a_dx": .61, "a_sil": .48,
        "a_u": .48, "a_da": .61, "a_cwh": .52, "a_xh": .52, "a_sp": 1.0, "a_win": .48, "a_xch": .52,
        "a_yh": .52, "a_acc": .48, "a_conv": .52, "a_dbl": .48}
LATE = 24

class Stream:

    load = {}

    def __init__(self, sem, step=1, name=""):
        self.sem, self.step, self.count = sem, step, 0
        self.engine, self.cost = name[0], COST.get(name, 0.0)

    def next(self):
        self.count += self.step
        self.load[self.engine] = self.load.get(self.engine, 0.0) + self.cost
        return (self.sem, self.count)

class Queue:

    def __init__(self):
        self.items, self.met = [], {}

    def wait(self, *marks):
        for m in marks:
            if m is None:
                continue
            sem, value = m
            if self.met.get(id(sem), 0) >= value:
                continue
            self.met[id(sem)] = value
            self.items.append(lambda e, sem=sem, value=value: e.wait_ge(sem, value))

    def do(self, fn, stream=None):
        if stream is None:
            self.items.append(fn)
            return None
        mark = stream.next()
        self.items.append(lambda e, fn=fn, sem=mark[0], k=stream.step: fn(e).then_inc(sem, k))
        return mark

    def play(self, eng):
        for f in self.items:
            f(eng)

def macaron_program(nc, x, W_in, conv_w, conv_b, W_x, W_dt, b_dt, A_log, D_param, W_out,
                    w_router, w_gating, w_gate, w_up, w_down, const, out):
    xf = x.rearrange("b (t j p) d -> (b t) p j d", t=2, j=SUB)
    of = out.rearrange("b (t j p) d -> (b t) p j d", t=2, j=SUB)

    with ExitStack() as ctx:
        def sb(name, shape, dt=F32):
            return ctx.enter_context(nc.sbuf_tensor(name, shape, dt))

        def stream(name, step=1):
            return Stream(ctx.enter_context(nc.semaphore(name)), step, name)

        WG = sb("WG", [P, 2, E, T], F32R)
        WU = sb("WU", [P, 2, E, T], F32R)
        WD = sb("WD", [P, E, FC, P])
        WI = sb("WI", [P, 2, T], F32R)
        WX = sb("WX", [P, 2, 2, 96], F32R)
        WT = sb("WT", [P, 2, 256], F32R)
        WO = sb("WO", [P, 2, 2, P], F32R)
        WR = sb("WR", [P, 16])
        CON = sb("CON", [P, P + NS * 2 + E])
        SEL = sb("SEL", [P, NS * 2 + E], F32R)
        cw_t = sb("cw_t", [P, 2, 4])
        cb_t = sb("cb_t", [P, 2])
        bdt_t = sb("bdt_t", [P, 2])
        d_t = sb("d_t", [P, 2])

        aneg = sb("aneg", [P, 2, NS])
        mhalf = sb("mhalf", [P, SUB])
        XT = sb("XT", [P, XR, SUB, P])
        XN = sb("XN", [P, SUB, P])
        XF = sb("XF", [P, 2, T])
        XH = sb("XH", [P, 2, 2, T], F32R)
        XC = sb("XC", [P, 2, 2, T], F32R)
        XCF = sb("XCF", [P, T])
        CW = sb("CW", [P, 2, T], F32R)
        HB = sb("HB", [P, NH, T])
        UB = sb("UB", [P, 2, T])
        stats = sb("stats", [P, SUB, 6])
        mv = sb("mv", [P, SUB, 2])
        rs = sb("rs", [P, SUB])
        ve = sb("ve", [P, SUB])
        lg = sb("lg", [P, SUB, 2, E])
        mx = sb("mx", [P, SUB, 2])
        zz = sb("zz", [P, SUB, 2])
        pq = sb("pq", [P, SUB, E])
        sm = sb("sm", [P, SUB])

        cwhl = sb("cwhl", [P, SUB, 2, E])
        RM = sb("RM", [P, 4, T], F32R)
        DTI = RM[:, 3, :]
        BC = sb("BC", [P, 2, T], F32R)
        XS = sb("XS", [P, 2, 2, T + 4])
        HT = sb("HT", [P, 2, 3])
        SZ = sb("SZ", [P, 2, 2, T])
        Y = sb("Y", [P, 2, 2, T])
        DX = sb("DX", [P, 2, 2, T])
        DA = sb("DA", [P, NA, 2, T])
        HS = sb("HS", [P, 3, 2, T])
        car = sb("car", [P, 2, NS])
        PS = ctx.enter_context(nc.psum_tensor("PS", [P, 8, T], F32))
        ident = CON[:, 0:P]

        S = {}
        load = Stream.load = {"v": 0.0, "p": 0.0, "a": 0.0}
        for n in ("c_small c_x0 c_x1 c_x2 c_x3 c_x4 "
                  "o_x0 o_x1 o_x2 o_x3 o_x4").split():
            S[n] = stream(n, 16)
        for e in range(E):
            for k in "gud":
                S[f"c_w{k}{e}"] = stream(f"c_w{k}{e}", 16)
        for n in ("init wh wl g u dn tz m_tr m_lg m_ct m_cb m_win m_wx m_wt m_b m_c m_wo "
                  "a_sil a_u a_cwh a_acc a_xh a_exp a_cwt a_win a_conv a_xch a_dbl a_sp a_da a_yh a_set a_xn a_xf a_cv a_dx "
                  "v_h v_g v_xcf v_ln v_xn v_xf v_sm v_cw v_add v_set v_halo v_z v_cv v_lo v_dt v_dx v_db v_sc v_car v_hc v_yz v_cwl "
                  "p_h p_cwl p_pow p_xl p_xcl p_y p_yl p_dx p_set").split():
            S[n] = stream(n)

        PE, VE, SC, GP, SY = (Queue() for _ in range(5))

        free_banks = [(0, ()), (1, ()), (2, ())]

        def bank():
            b, marks = free_banks.pop(0)
            PE.wait(*marks)
            return b, PS[:, 5 + b, :]

        def release(b, *marks):
            free_banks.append((b, marks))

        def mm(outp, terms, s):
            mark = None
            for k, (l, r) in enumerate(terms):
                first, last = k == 0, k == len(terms) - 1
                mark = PE.do(lambda e, l=l, r=r, f=first, z=last: e.matmul(outp, l, r, start=f, stop=z),
                             S[s] if last else None)
            return mark

        def tt(q, o, a, b, op, s):
            return q.do(lambda e: e.tensor_tensor(o, a, b, op), S[s])

        def ts(q, o, a, s1, s2, op0, op1, s):
            if op1 is None:
                return q.do(lambda e: e.tensor_scalar(o, a, s1, None, op0), S[s])
            return q.do(lambda e: e.tensor_scalar(o, a, s1, s2, op0, op1), S[s])

        def act(o, a, f, s, **kw):
            return SC.do(lambda e: e.activation(o, a, f, **kw), S[s])

        def f32(ap):
            return ap.bitcast(F32)

        XTfree = [[] for _ in range(XR)]

        def load_x(t):
            b = t % XR
            SY.wait(*XTfree[b])
            return SY.do(lambda e: e.dma_start(XT[:, b, :, :], xf[t]), S[f"c_x{b}"])

        x_in = {0: load_x(0)}
        small = None
        stI = DA[:, 0, 0, :]
        stX = DA[:, 0, 1, 0:192].rearrange("p (k n) -> p k n", k=2)
        stT = DA[:, 0, 1, 192:448]
        stO = DA[:, 1, 0, 0:256].rearrange("p (k n) -> p k n", k=2)
        for dst, src in ((CON[:, :], const), (WR[:, 0:E], w_router), (WR[:, E:2 * E], w_gating)):
            small = SY.do(lambda e, dst=dst, src=src: e.dma_start(dst, src), S["c_small"])
        first_small = small

        def stage(e, k):
            return (HS[:, 0, k, :], HS[:, 1, k, :], HS[:, 2, k, :], DX[:, 1, k, :])[e % 4]

        st_free = {}
        w_in_mark = {}

        def load_w(e):
            for k, (n, src) in enumerate((("g", w_gate[e]), ("u", w_up[e]))):
                SY.wait(st_free.get((e - 4, k)))
                dst = stage(e, k)
                w_in_mark[e, k] = SY.do(lambda q, dst=dst, src=src: q.dma_start(dst, src), S[f"c_w{n}{e}"])
            src = w_down[e].rearrange("(c p) n -> p c n", p=P)
            w_mark[e, 2] = SY.do(lambda q: q.dma_start(WD[:, e, :, :], src), S[f"c_wd{e}"])

        w_mark = {}

        def split_w(e):
            for k, W in enumerate((WG, WU)):
                src = stage(e, k)
                hi, lo = W[:, 0, e, :], W[:, 1, e, :]
                SC.wait(w_in_mark[e, k])
                h = act(hi, src, ACT.Copy, "wh")
                VE.wait(h, w_in_mark[e, k])
                w_mark[e, k] = tt(VE, lo, src, f32(hi), ALU.subtract, "wl")
                st_free[e, k] = w_mark[e, k]

        for e in range(4):
            load_w(e)

        def load_small():
            nonlocal small
            loads = [(stI, W_in), (stX, W_x.rearrange("(k p) n -> p k n", p=P)),
                     (stT[0:RT, :], W_dt), (stT[RT:2 * RT, :], W_dt),
                     (stO, W_out.rearrange("(k p) n -> p k n", p=P)),
                     (cw_t[:, :, :], conv_w.rearrange("(k p) n -> p k n", p=P)),
                     (aneg[:, :, :], A_log.rearrange("(k p) n -> p k n", p=P))]
            for dst, v in ((cb_t, conv_b), (bdt_t, b_dt), (d_t, D_param)):
                loads += [(dst[:, k:k + 1], v.rearrange("(k p o) -> k p o", p=P, o=1)[k]) for k in range(2)]
            for dst, src in loads:
                small = SY.do(lambda e, dst=dst, src=src: e.dma_start(dst, src), S["c_small"])

        VE.do(lambda e: e.memset(mhalf[:, :], -0.5), S["init"])
        VE.do(lambda e: e.memset(f32(BC[0:64, :, :]), 0.0), S["init"])
        init = VE.do(lambda e: e.memset(f32(CW[:, :, :]), 0.0), S["init"])
        sel = []

        def selectors():
            VE.wait(first_small)
            sel.append( VE.do(lambda e: e.tensor_copy(SEL[:, :], CON[:, P:P + 2 * NS + E]), S["init"]))

        def setup_mamba():
            VE.wait(small)
            for hi, lo, src in ((WI[:, 0, :], WI[:, 1, :], stI), (WX[:, :, 0, :], WX[:, :, 1, :], stX),
                                (WT[:, 0, :], WT[:, 1, :], stT), (WO[:, :, 0, :], WO[:, :, 1, :], stO)):
                h = VE.do(lambda q, hi=hi, src=src: q.tensor_copy(hi, src), S["v_set"])
                VE.wait(h)
                l = tt(VE, lo, src, f32(hi), ALU.subtract, "v_set")
                yield
            ts(VE, cb_t[:, :], cb_t[:, :], 0.5, None, ALU.mult, None, "v_set")
            ts(VE, cw_t[:, :, :], cw_t[:, :, :], 0.5, None, ALU.mult, None, "v_set")
            SC.wait(small)
            a = act(aneg[:, :, :], aneg[:, :, :], ACT.Exp, "a_set")
            VE.wait(a)
            st["m_ready"] = ts(VE, aneg[:, :, :], aneg[:, :, :], -1.0, None, ALU.mult, None, "v_set")
            yield

        st = {}
        XNfree = [None]
        lock = [False]
        xn_lock = [False]
        tiny = {}

        def norm_transposed(b, xmark):
            while lock[0]:
                yield
            lock[0] = True
            VE.wait(*xmark)
            for j in range(SUB):
                m = VE.do(lambda e, j=j: e.bn_stats(stats[:, j, :], XT[:, b, j, :]), S["v_ln"])
            VE.wait(m)
            for j in range(SUB):
                m = VE.do(lambda e, j=j: e.bn_aggr(mv[:, j, :], stats[:, j, :]), S["v_ln"])
            VE.wait(m)
            m = ts(VE, ve[:, :], mv[:, :, 1], EPS_LN, None, ALU.add, None, "v_ln")
            GP.wait(m, init, tiny.get("rs"))
            m = tt(GP, rs[:, :], ve[:, :], mhalf[:, :], ALU.pow, "p_pow")
            yield
            yield
            while xn_lock[0]:
                yield
            xn_lock[0] = True
            VE.wait(m, XNfree[0])
            for j in range(SUB):
                m = VE.do(lambda e, j=j: e.tensor_scalar(XN[:, j, :], XT[:, b, j, :], mv[:, j, 0:1], rs[:, j:j + 1],
                                                         ALU.subtract, ALU.mult), S["v_xn"])
            lock[0] = False
            yield
            yield
            while len(free_banks) < 1:
                yield
            bk, ps = bank()
            PE.wait(m, first_small)
            for j in range(SUB):
                t = PE.do(lambda e, j=j: e.transpose(ps[:, j * P:(j + 1) * P], XN[:, j, :], ident), S["m_tr"])
            XNfree[0] = t
            xn_lock[0] = False
            yield
            return bk, ps, t

        prepared = {}
        parts = {}
        xh_free = [None, None]
        xf_free = [None, None]
        cw_free = [None, None]

        def prep(p, b, xmark):
            k = p % 2
            bk, ps, t = yield from norm_transposed(b, xmark)
            SC.wait(t, xf_free[k])
            mf = act(XF[:, k, :], ps, ACT.Copy, "a_xf")
            release(bk, mf)
            yield
            SC.wait(mf, xh_free[k])
            mh = act(XH[:, k, 0, :], XF[:, k, :], ACT.Copy, "a_xh")
            GP.wait(mh, mf)
            ml = tt(GP, XH[:, k, 1, :], XF[:, k, :], f32(XH[:, k, 0, :]), ALU.subtract, "p_xl")
            parts[p] = (mh, ml)
            yield
            while len(free_banks) < 1:
                yield
            bk, ps = bank()
            PE.wait(mf)
            for j in range(SUB):
                t = PE.do(lambda e, j=j, ps=ps: e.matmul(ps[:, j * 16:j * 16 + 16], XF[:, k, j * P:(j + 1) * P], WR[:, :],
                                                         start=True, stop=True), S["m_lg"])
            yield "logits"
            l4 = ps[:, 0:SUB * 16].rearrange("p (j g e) -> p j g e", j=SUB, g=2)
            VE.wait(t)
            m = VE.do(lambda e: e.tensor_reduce(mx[:, :, :], l4, AX.X, ALU.max), S["v_sm"])
            VE.wait(m)
            m = tt(VE, lg[:, :, :, :], l4, mx[:, :, :].unsqueeze(3).broadcast_to([P, SUB, 2, E]), ALU.subtract, "v_sm")
            release(bk, m)
            yield
            SC.wait(m)
            act(lg[:, :, 0, :], lg[:, :, 0, :], ACT.Exp, "a_exp")
            m = act(lg[:, :, 1, :], lg[:, :, 1, :], ACT.Exp, "a_exp", scale=10.0)
            yield
            VE.wait(m)
            m = VE.do(lambda e: e.tensor_reduce(zz[:, :, :], lg[:, :, :, :], AX.X, ALU.add), S["v_sm"])
            VE.wait(m)
            m = VE.do(lambda e: e.reciprocal(zz[:, :, :], zz[:, :, :]), S["v_sm"])
            VE.wait(m)
            m = tt(VE, lg[:, :, :, :], lg[:, :, :, :], zz[:, :, :].unsqueeze(3).broadcast_to([P, SUB, 2, E]), ALU.mult, "v_sm")
            yield
            VE.wait(m)
            m = tt(VE, pq[:, :, :], lg[:, :, 0, :], lg[:, :, 1, :], ALU.mult, "v_sm")
            VE.wait(m)
            m = VE.do(lambda e: e.tensor_reduce(sm[:, :], pq[:, :, :], AX.X, ALU.add), S["v_sm"])
            VE.wait(m)
            m = ts(VE, sm[:, :], sm[:, :], EPS_CW, 2.0, ALU.add, ALU.mult, "v_sm")
            yield
            VE.wait(m)
            m = VE.do(lambda e: e.reciprocal(sm[:, :], sm[:, :]), S["v_sm"])
            VE.wait(m)
            m = tt(VE, pq[:, :, :], pq[:, :, :], sm[:, :].unsqueeze(2).broadcast_to([P, SUB, E]), ALU.mult, "v_sm")
            yield
            VE.wait(m, tiny.get("cwhl"))
            m = VE.do(lambda e: e.tensor_copy(cwhl[:, :, 0, :].bitcast(F32R), pq[:, :, :]), S["v_sm"])
            VE.wait(m)
            m = tt(VE, cwhl[:, :, 1, :].bitcast(F32R), pq[:, :, :], cwhl[:, :, 0, :], ALU.subtract, "v_cw")
            yield
            while len(free_banks) < 1:
                yield
            bk, ps = bank()
            PE.wait(m)
            for j in range(SUB):
                t = PE.do(lambda e, j=j, ps=ps: e.transpose(ps[0:16, j * P:(j + 1) * P],
                                                            cwhl[:, j, :, :].rearrange("p g e -> p (g e)"), ident), S["m_ct"])
            tiny["cwhl"] = t
            yield
            SC.wait(t, cw_free[k], init)
            m = act(CW[0:16, k, :], ps[0:16, :], ACT.Copy, "a_cwt")
            release(bk, m)
            prepared[p] = (mh, ml, m)
            yield

        xc_free = [None, None]
        xc_mark = {}
        xcf_free = [None]

        def scale_x(g):
            p, e = divmod(g, E)
            k, b2 = p % 2, g % 2
            while len(free_banks) < 1:
                yield
            bk, ps = bank()
            PE.wait(prepared[p][2], sel[0])
            t = PE.do(lambda q: q.matmul(ps, SEL[:, 2 * NS + e:2 * NS + e + 1].broadcast_to([P, P]), CW[:, k, :],
                                         start=True, stop=True), S["m_cb"])
            cw_free[k] = t
            VE.wait(t, xcf_free[0])
            m = tt(VE, XCF[:, :], ps, XF[:, k, :], ALU.mult, "v_xcf")
            release(bk, m)
            xf_free[k] = m
            yield
            SC.wait(m, xc_free[b2])
            h = act(XC[:, b2, 0, :], XCF[:, :], ACT.Copy, "a_cwh")
            q, s = (VE, "v_cwl") if g == 0 or load["p"] > XLIM and load["p"] > load["v"] + DIFF else (GP, "p_cwl")
            q.wait(h, m, xc_free[b2])
            l = tt(q, XC[:, b2, 1, :], XCF[:, :], f32(XC[:, b2, 0, :]), ALU.subtract, s)
            xcf_free[0] = l
            xc_mark[g] = (h, l)
            yield

        hist = {}
        acc_free = [None]
        acc_done = set()
        ub_free, ub_n = [None, None], [0]

        def tail(p):
            kind, t = ORDER[p]
            b = t % XR
            while xn_lock[0]:
                yield
            xn_lock[0] = True
            SC.wait(hist[p * SLOTS + SLOTS - 1]["dn"], XNfree[0])
            A = XN[:, :, :].rearrange("p j d -> p (j d)")
            m = act(A, PS[:, 4, :], ACT.Copy, "a_acc")
            acc_free[0] = m
            acc_done.add(p)
            yield
            while len(free_banks) < 1:
                yield
            bk, ps = bank()
            PE.wait(m)
            for j in range(SUB):
                tr = PE.do(lambda e, j=j: e.transpose(ps[:, j * P:(j + 1) * P], A[:, j * P:(j + 1) * P], ident), S["tz"])
            XNfree[0] = tr
            xn_lock[0] = False
            yield
            VE.wait(tr)
            m = tt(VE, XT[:, b, :, :].rearrange("p j d -> p (j d)"), XT[:, b, :, :].rearrange("p j d -> p (j d)"),
                   ps, ALU.add, "v_add")
            release(bk, m)
            if kind == 0:
                st["x1", t] = m
            else:
                SY.wait(m)
                o = SY.do(lambda e: e.dma_start(of[t], XT[:, b, :, :]), S[f"o_x{b}"])
                XTfree[b] = [o]
                outs.append(o)
            yield

        outs = []

        def first_g(i):
            p, r = divmod(i, SLOTS)
            e, c = divmod(r, FC)
            k = p % 2
            h = hist.setdefault(i, {})
            wg = [WG[:, s, e, c * P:(c + 1) * P] for s in (0, 1)]
            PE.wait(w_mark[e, 0], *parts[p])
            if i - 2 in hist:
                PE.wait(hist[i - 2]["sil"])
            xh, xl = XH[:, k, 0, :], XH[:, k, 1, :]
            h["g"] = mm(PS[:, i % 2, :], [(wg[0], xh), (wg[0], xl), (wg[1], xh)], "g")
            xh_free[k] = h["g"]

        def first(i):
            if i > 1:
                first_g(i)
            p, r = divmod(i, SLOTS)
            e, c = divmod(r, FC)
            k = p % 2
            G, U = PS[:, i % 2, :], PS[:, 2 + i % 2, :]
            h, old = hist[i], hist.get(i - 2)
            wu = [WU[:, s, e, c * P:(c + 1) * P] for s in (0, 1)]
            PE.wait(w_mark[e, 1])
            b2 = (p * E + e) % 2
            PE.wait(*xc_mark[p * E + e])
            if old:
                PE.wait(old["uf"])
            xh, xl = XC[:, b2, 0, :], XC[:, b2, 1, :]
            h["u"] = mm(U, [(wu[0], xh), (wu[0], xl), (wu[1], xh)], "u")
            xc_free[b2] = h["u"]
            H, B = HB[:, i % NH, :], UB[:, ub_n[0] % 2, :]
            if i >= NH:
                SC.wait(hist[i - NH]["dn"])
            SC.wait(h["g"])
            if p in PLAIN:
                h["sil"] = act(H, G, ACT.Silu, "a_sil")
                VE.wait(h["sil"], h["u"])
                h["h"] = h["uf"] = tt(VE, H, U, H, ALU.mult, "v_h")
            else:
                a = act(H, G, ACT.Tanh, "a_sil", scale=0.5)
                VE.wait(a)
                h["sil"] = VE.do(lambda q: q.scalar_tensor_tensor(out=H, in0=H, scalar=1.0, in1=G, op0=ALU.add,
                                                                  op1=ALU.mult), S["v_g"])
                if load["p"] > PLIM and load["p"] > load["v"] + DIFF:
                    VE.wait(h["sil"], h["u"])
                    h["h"] = h["uf"] = VE.do(lambda q: q.scalar_tensor_tensor(out=H, in0=H, scalar=0.5, in1=U,
                                                                             op0=ALU.mult, op1=ALU.mult), S["v_h"])
                    return
                SC.wait(h["u"], ub_free[0])
                ub_free[0] = ub_free[1]
                ub_n[0] += 1
                h["uf"] = act(B, U, ACT.Copy, "a_u", scale=0.5)
                GP.wait(h["sil"], h["uf"])
                h["h"] = tt(GP, H, H, B, ALU.mult, "p_h")
                ub_free[1] = h["h"]

        def down(i):
            p, r = divmod(i, SLOTS)
            e, c = divmod(r, FC)
            h = hist[i]
            H = HB[:, i % NH, :]
            if r == 0:
                PE.wait(acc_free[0])
            PE.wait(w_mark[e, 2], h["h"])
            h["dn"] = PE.do(lambda q: q.matmul(PS[:, 4, :], WD[:, e, c, :], H, start=r == 0, stop=r == SLOTS - 1), S["dn"])

        mfree = {}
        ready = {}
        rm_lock = [False]

        def before(t):
            b, v = t % XR, t % 2
            start = t % 2 == 0
            xs, y, dx, sz = XS[:, v, :, :], Y[:, v, :, :], DX[:, v, :, :], SZ[:, v, :, :]
            if t == 0:
                yield from setup_mamba()
                PE.wait(st["m_ready"])
                SC.wait(st["m_ready"])
            while rm_lock[0]:
                yield
            rm_lock[0] = True
            bk, ps, tr = yield from norm_transposed(b, [st["x1", t]])
            SC.wait(tr, mfree.get("RM"))
            mh = act(RM[:, 0, :], ps, ACT.Copy, "a_xh")
            VE.wait(mh, tr)
            ml = tt(VE, RM[:, 1, :], ps, f32(RM[:, 0, :]), ALU.subtract, "v_lo")
            release(bk, mh, ml)
            if start:
                VE.wait(mfree.get(("XS", v)))
                ch = VE.do(lambda e: e.memset(xs[:, :, 0:3], 0.0), S["v_halo"])
            else:
                VE.wait(mfree.get(("XS", v)))
                ch = VE.do(lambda e: e.tensor_copy(xs[:, :, 0:3], HT[:, :, :]), S["v_halo"])
            yield
            yield
            for j in range(4):
                while len(free_banks) < 2:
                    yield
                bk, ps = bank()
                PE.wait(mh, ml)
                w = [WI[:, s, j * P:(j + 1) * P] for s in (0, 1)]
                tm = mm(ps, [(w[0], RM[:, 0, :]), (w[0], RM[:, 1, :]), (w[1], RM[:, 0, :])], "m_win")
                SC.wait(tm)
                if j < 2:
                    SC.wait(mfree.get(("XS", v)))
                    m = act(xs[:, j, 3:3 + T], ps, ACT.Copy, "a_win")
                    xs_m = m
                else:
                    SC.wait(mfree.get(("SZ", v)))
                    a = act(sz[:, j - 2, :], ps, ACT.Tanh, "a_win", scale=0.5)
                    VE.wait(a)
                    m = VE.do(lambda e, j=j, ps=ps: e.scalar_tensor_tensor(
                        out=sz[:, j - 2, :], in0=sz[:, j - 2, :], scalar=1.0, in1=ps, op0=ALU.add, op1=ALU.mult), S["v_z"])
                release(bk, m)
                yield
            sz_m = m
            VE.wait(xs_m, ch)
            VE.do(lambda e: e.tensor_copy(HT[:, :, :], xs[:, :, T:T + 3]), S["v_halo"])
            VE.wait(mfree.get(("Y", v)))
            cm = [None, None]
            for q in range(4):
                for j in range(2):
                    if q == 0:
                        cm[j] = ts(VE, y[:, j, :], xs[:, j, 0:T], cw_t[:, j, 0:1], cb_t[:, j:j + 1], ALU.mult,
                                   ALU.add, "v_cv")
                    else:
                        VE.wait(cm[j])
                        cm[j] = VE.do(lambda e, j=j, q=q: e.scalar_tensor_tensor(
                            out=y[:, j, :], in0=xs[:, j, q:q + T], scalar=cw_t[:, j, q:q + 1], in1=y[:, j, :],
                            op0=ALU.mult, op1=ALU.add), S["v_cv"])
                yield
            xcm, tx = [], tm
            for j in range(2):
                SC.wait(cm[j], mfree.get(("DX", v)))
                a = act(dx[:, j, :], y[:, j, :], ACT.Tanh, "a_conv")
                VE.wait(a)
                m = VE.do(lambda e, j=j: e.scalar_tensor_tensor(
                    out=y[:, j, :], in0=dx[:, j, :], scalar=1.0, in1=y[:, j, :], op0=ALU.add, op1=ALU.mult), S["v_cv"])
                SC.wait(m, tx)
                mh = act(RM[:, 2 * j, :], y[:, j, :], ACT.Copy, "a_xch")
                GP.wait(m, mh, tx)
                ml = tt(GP, RM[:, 2 * j + 1, :], y[:, j, :], f32(RM[:, 2 * j, :]), ALU.subtract, "p_xcl")
                xcm.append(m)
                for _ in range((0, 2)[j]):
                    yield
            while len(free_banks) < 2:
                yield
            bk, ps = bank()
            PE.wait(mh, ml)
            terms = []
            for j in range(2):
                w = [WX[:, j, s, :] for s in (0, 1)]
                terms += [(w[0], RM[:, 2 * j, :]), (w[0], RM[:, 2 * j + 1, :]), (w[1], RM[:, 2 * j, :])]
            tm = mm(ps[0:96, :], terms, "m_wx")
            SC.wait(tm, mfree.get(("BC", v)))
            bc = BC[:, v, :]
            m1 = act(DTI[0:RT, :], ps[0:RT, :], ACT.Copy, "a_dbl")
            m2 = act(bc[64:96, :], ps[64:96, :], ACT.Copy, "a_dbl")
            VE.wait(m1, m2, tm)
            m3 = tt(VE, DTI[RT:2 * RT, :], ps[0:RT, :], f32(DTI[0:RT, :]), ALU.subtract, "v_lo")
            m4 = tt(VE, bc[96:128, :], ps[64:96, :], f32(bc[64:96, :]), ALU.subtract, "v_lo")
            release(bk, m2, m4)
            yield
            yield
            pend = []
            for j in range(2):
                while len(free_banks) < 2:
                    yield
                bk, ps = bank()
                PE.wait(m1, m3)
                tm = mm(ps, [(WT[:, s, j * P:(j + 1) * P], DTI) for s in (0, 1)], "m_wt")
                SC.wait(tm, mfree.get(("DX", v)))
                a = act(dx[:, j, :], ps, ACT.Abs, "a_sp", bias=bdt_t[:, j:j + 1])
                VE.wait(tm, a)
                r = act(xs[:, j, 3:3 + T], ps, ACT.Relu, "a_sp", bias=bdt_t[:, j:j + 1])
                release(bk, a, r)
                pend.append((a, r))
                yield
            mfree["RM"] = tm
            rm_lock[0] = False
            SC.wait(pend[1][0])
            a = act(dx, dx, ACT.Exp, "a_sp", scale=-1.0)
            SC.wait(a)
            a = act(dx, dx, ACT.Ln, "a_sp", bias=1.0)
            yield
            VE.wait(a, pend[1][1])
            dt = xs[:, :, 3:3 + T]
            dtm = tt(VE, dt, dt, dx, ALU.add, "v_dt")
            GP.wait(dtm, *xcm)
            dxm = tt(GP, dx, dt, y, ALU.mult, "p_dx")
            yield
            VE.wait(dxm)
            for j in range(2):
                ym = ts(VE, y[:, j, :], y[:, j, :], d_t[:, j:j + 1], None, ALU.mult, None, "v_dx")
            ready[t] = (dtm, dxm, ym, sz_m, m2, m4)
            yield

        def scans(t):
            b, v = t % XR, t % 2
            xs, y, dx, sz, bc = XS[:, v, :, :], Y[:, v, :, :], DX[:, v, :, :], SZ[:, v, :, :], BC[:, v, :]
            dtm, dxm, ym, sz_m, m2, m4 = ready[t]
            da, hb = {}, {}

            def decay(n):
                SC.wait(dtm, mfree.get(("DA", n % NA)))
                for j in range(2):
                    m = act(DA[:, n % NA, j, :], xs[:, j, 3:3 + T], ACT.Exp, "a_da", scale=aneg[:, j, n:n + 1])
                da[n] = m

            def spread(n, col):
                bb, pb = bank()
                PE.wait(m2, m4)
                m = PE.do(lambda e: e.matmul(pb, SEL[:, col:col + 1].broadcast_to([P, P]), bc, start=True, stop=True),
                          S["m_b"])
                return bb, pb, m

            def enter(n):
                while len(free_banks) < 2:
                    yield -1.0
                bb, pb, tb = spread(n, n)
                H = HS[:, n % 3, :, :]
                VE.wait(tb, dxm, mfree.get(("HS", n % 3)))
                m = tt(VE, H, pb.unsqueeze(1).broadcast_to([P, 2, T]), dx, ALU.mult, "v_db")
                release(bb, m)
                hb[n] = m

            for n in range(2):
                decay(n)
                yield from enter(n)
                yield 1.0
            for n in range(NS):
                H = HS[:, n % 3, :, :]
                VE.wait(hb[n], da[n])
                for j in range(2):
                    m = VE.do(lambda e, n=n, j=j, H=H: e.tensor_tensor_scan(
                        H[:, j, :], DA[:, n % NA, j, :], H[:, j, :], car[:, j, n:n + 1] if t % 2 else 0.0, ALU.mult, ALU.add), S["v_sc"])
                mfree["DA", n % NA] = m
                while len(free_banks) < 2:
                    yield -1.0
                bb, pb, tb = spread(n, NS + n)
                yield 1.2
                VE.wait(m, tb)
                if t % 2 == 0:
                    cm = VE.do(lambda e, n=n, H=H: e.tensor_copy(car[:, :, n], H[:, :, T - 1]), S["v_car"])
                    VE.wait(cm)
                m = tt(VE, H, pb.unsqueeze(1).broadcast_to([P, 2, T]), H, ALU.mult, "v_hc")
                release(bb, m)
                GP.wait(m, ym)
                for j in range(2):
                    ym = tt(GP, y[:, j, :], y[:, j, :], H[:, j, :], ALU.add, "p_y")
                mfree["HS", n % 3] = ym
                yield 1.2
                if n + 2 < NS:
                    decay(n + 2)
                if n + 2 < NS:
                    yield from enter(n + 2)
                    yield 1.2
            mfree["BC", v] = tb
            mfree["XS", v] = da[NS - 1]
            mfree["DX", v] = hb[NS - 1]
            yield 3.0
            VE.wait(ym, sz_m)
            m = VE.do(lambda e: e.scalar_tensor_tensor(out=y, in0=y, scalar=0.5, in1=sz, op0=ALU.mult, op1=ALU.mult),
                      S["v_yz"])
            mfree["SZ", v] = m
            yield 1.5
            while rm_lock[0]:
                yield 1.5
            SC.wait(m)
            for j in range(2):
                SC.wait(mfree["RM"])
                GP.wait(mfree["RM"])
                mh = act(RM[:, 2 * j, :], y[:, j, :], ACT.Copy, "a_yh")
                GP.wait(mh, m)
                ml = tt(GP, RM[:, 2 * j + 1, :], y[:, j, :], f32(RM[:, 2 * j, :]), ALU.subtract, "p_yl")
            rm_lock[0] = True
            yield 3.0
            mfree["Y", v] = ml
            while len(free_banks) < 2:
                yield -1.0
            bk, ps = bank()
            PE.wait(mh, ml)
            for s4 in range(SUB):
                terms = []
                for j in range(2):
                    yh = RM[:, 2 * j, s4 * P:(s4 + 1) * P]
                    yl = RM[:, 2 * j + 1, s4 * P:(s4 + 1) * P]
                    terms += [(yh, WO[:, j, 0, :]), (yl, WO[:, j, 0, :]), (yh, WO[:, j, 1, :])]
                tm = mm(ps[:, s4 * P:(s4 + 1) * P], terms, "m_wo")
            mfree["RM"] = tm
            rm_lock[0] = False
            yield 1.5
            VE.wait(tm)
            X = XT[:, b, :, :].rearrange("p j d -> p (j d)")
            m = tt(VE, X, X, ps, ALU.add, "v_add")
            release(bk, m)
            st["x2", t] = m
            yield 0.0

        def run(gen, n=10 ** 9):
            for _ in range(n):
                if next(gen, "end") == "end":
                    return True
            return False

        def xmark(p):
            kind, t = ORDER[p]
            return [x_in[t]] if kind == 0 else [st["x2", t]]

        opening = prep(0, 0, [x_in[0]])
        while next(opening) != "logits":
            pass
        split_w(0)
        selectors()
        first_g(0)
        first_g(1)
        run(opening)
        run(scale_x(0))
        total = NPOS * SLOTS
        nd = [0]
        started = set()
        side = {"b": None, "bt": 0, "s": None, "stt": 0, "cost": 0.0, "pace": 0.0}

        def step_before():
            if side["b"] is None:
                t = side["bt"]
                if t >= NT or ("x1", t) not in st or t > side["stt"] + 1:
                    return False
                side["b"] = before(t)
            if next(side["b"], "end") == "end":
                side["b"] = None
                side["bt"] += 1
            return True

        def step_scans():
            if side["s"] is None:
                t = side["stt"]
                if t >= NT or t not in ready:
                    return None
                side["s"] = scans(t)
            w = next(side["s"], "end")
            if w == "end":
                side["s"] = None
                side["stt"] += 1
                return 0.0
            return 0.5 if w is None else w

        gens = {"tail": None, "x": None, "prep": None}

        def step(k):
            if gens[k] is not None and next(gens[k], "end") == "end":
                gens[k] = None

        def others(k):
            for o in gens:
                if o != k:
                    step(o)
            step_before()
            if k != "x":
                step_scans()

        def finish(k):
            while gens[k] is not None:
                step(k)
                if gens[k] is not None and (k != "x" or not free_banks):
                    others(k)

        for i in range(total):
            p, r = divmod(i, SLOTS)
            for k in load:
                load[k] = max(0.0, load[k] - SLOT_WEIGHT)
            first(i)
            while nd[0] <= i - LAG:
                d = nd[0]
                if d % SLOTS == 0 and d:
                    while d // SLOTS - 1 not in acc_done:
                        step("tail")
                        if d // SLOTS - 1 not in acc_done:
                            others("tail")
                down(d)
                nd[0] += 1
                if nd[0] % SLOTS == 0:
                    gens["tail"] = tail(nd[0] // SLOTS - 1)
            if p == 0:
                if r % 4 == 0 and r // 4 + 1 < E:
                    split_w(r // 4 + 1)
                    if r // 4 + 4 < E:
                        load_w(r // 4 + 4)
                if r == 6:
                    load_small()
            if r == LOADR and p + 1 < NPOS and ORDER[p + 1][0] == 0:
                t = ORDER[p + 1][1]
                x_in[t] = load_x(t)
            if r % 4 == 1:
                finish("x")
            if r % 4 == 0 and i // 4 + 1 < NPOS * E:
                if r // 4 == E - 1:
                    finish("prep")
                gens["x"] = scale_x(i // 4 + 1)
                step("x")
            step("tail")
            side["pace"] = min(side["pace"] + BRATE, 2.0)
            if i >= BEGIN and side["pace"] >= 1.0:
                step_before()
                side["pace"] -= 1.0
            side["cost"] = min(side["cost"] + RATE, MAXC)
            while side["cost"] > 0:
                w = step_scans()
                if w is None or w < 0:
                    break
                side["cost"] -= w
            if p + 1 < NPOS and r >= PREP and p + 1 not in started:
                kind, t = ORDER[p + 1]
                if kind == 1 and r == LATE:
                    while ("x2", t) not in st:
                        others("prep")
                if kind == 0 or ("x2", t) in st:
                    gens["prep"] = prep(p + 1, t % XR, xmark(p + 1))
                    started.add(p + 1)
            step("prep")
        for i in range(nd[0], total):
            down(i)
        run(tail(NPOS - 1))
        for o in outs:
            SY.wait(o)

        block = ctx.enter_context(nc.Block())

        @block.sync
        def _(eng):
            SY.play(eng)

        @block.tensor
        def _(eng):
            PE.play(eng)

        @block.vector
        def _(eng):
            VE.play(eng)

        @block.scalar
        def _(eng):
            SC.play(eng)

        @block.gpsimd
        def _(eng):
            GP.play(eng)

_INS = ['L0_attn_x', 'L0_attn_W_in', 'L0_attn_conv_w', 'L0_attn_conv_b', 'L0_attn_W_x', 'L0_attn_W_dt', 'L0_attn_b_dt',
        'L0_attn_A_log', 'L0_attn_D_param', 'L0_attn_W_out', 'L0_ffn_w_router', 'L0_ffn_w_gating', 'L0_ffn_w_gate',
        'L0_ffn_w_up', 'L0_ffn_w_down']

def _constants():
    c = np.zeros((P, P + 2 * NS + E), np.float32)
    c[:, :P] = np.eye(P)
    for n in range(2 * NS):
        c[64 + n, P + n] = 1.0
        c[96 + n, P + n] = 1.0
    for e in range(E):
        c[e, P + 2 * NS + e] = 1.0
        c[E + e, P + 2 * NS + e] = 1.0
    return c

def kernel(**inputs):
    import concourse.bacc as _bacc
    from concourse.bass_utils import run_bass_kernel_spmd as _run

    nc = _bacc.Bacc("TRN2", target_bir_lowering=False, num_devices=1)
    arrays, args = {}, []
    for name in _INS:
        a = np.ascontiguousarray(inputs[name])
        arrays[f"in_{name}_dram"] = a
        args.append(nc.dram_tensor(f"in_{name}_dram", a.shape, mybir.dt.from_np(a.dtype), kind="ExternalInput").ap())
    c = _constants()
    arrays["in_const_dram"] = c
    args.append(nc.dram_tensor("in_const_dram", c.shape, F32, kind="ExternalInput").ap())
    args.append(nc.dram_tensor("out_0_dram", (4, 1024, P), F32, kind="ExternalOutput").ap())
    macaron_program(nc, *args)
    r = _run(nc, [arrays], core_ids=[0])
    return r.results[0]["out_0_dram"]
```
